# Optimizing a Trainium2 kernel written in Bass

```python
import numpy as np
import jax
import jax.numpy as jnp

def _softmax(x, axis=-1):
    return jax.nn.softmax(x, axis=axis)

def _gelu(x):
    return jax.nn.gelu(x, approximate=True)

def _silu(x):
    return jax.nn.silu(x)

def _sigmoid(x):
    return jax.nn.sigmoid(x)

def _layernorm(x, axis=-1, eps=1e-05):
    m = jnp.mean(x, axis=axis, keepdims=True)
    v = jnp.var(x, axis=axis, keepdims=True)
    return (x - m) / jnp.sqrt(v + eps)

def _scatter_add(tgt, idx, src, axis=0):
    return tgt.at[idx].add(src)

def _segment_sum(src, seg, n):
    return jax.ops.segment_sum(src, seg, n)
kernel_name = 'mk_adaln_ffn_d1_seqx_r4_dd4f9b'

def setup_inputs(seed: int=0):
    np.random.seed(seed)
    _w = jnp.asarray

    def _rec_inputs():
        import jax
        import jax.numpy as jnp
        _rk = jax.random.key(seed)
        x = -0.000125 + 0.9999 * jax.random.normal(jax.random.fold_in(_rk, 1), (8, 256, 1024), jnp.float32)
        _lenS = 256 - jax.random.randint(jax.random.fold_in(_rk, 7), (8,), 0, max(1, 256 // 4) + 1, jnp.int32)
        _lenS2 = 256 - jax.random.randint(jax.random.fold_in(_rk, 8), (8,), 0, max(1, 256 // 4) + 1, jnp.int32)
        itok_B_3_7 = jax.random.randint(jax.random.fold_in(_rk, 11), (8,), 3, 8, jnp.int32)
        return (x, itok_B_3_7)
    x, itok_B_3_7 = _rec_inputs()

    def _L0_cond_setup():
        import jax, jax.numpy as jnp
        import numpy as np
        MAX_LORAS, OUT, IN = (8, 1024, 1024)
        B, S = (4, 512)
        key = jax.random.key(seed)
        k1, k2, k3 = jax.random.split(key, 3)
        x = jax.random.normal(k1, (B, S, IN), dtype=jnp.float32)
        weight = jax.random.normal(k2, (MAX_LORAS, OUT, IN), dtype=jnp.float32) * 0.02
        adapter_ids = jax.random.randint(k3, (B,), 0, MAX_LORAS, dtype=jnp.int32)
        return {'x': x, 'weight': weight, 'adapter_ids': adapter_ids}
    _L0_cond_all = _L0_cond_setup()
    _L0_cond_in = {k: v for k, v in _L0_cond_all.items() if k in ('weight',)}
    del _L0_cond_all

    def _L0_ffn_setup():
        import jax, jax.numpy as jnp
        import numpy as np
        D_IN = 1024
        D_OUT = 1024
        RANK = 16
        NUM_EXPERTS = 8
        TOP_K = 2
        SCALING = 32.0 / RANK
        key = jax.random.key(seed)
        ks = jax.random.split(key, 6)
        x = jax.random.normal(ks[0], (4, 512, D_IN), dtype=jnp.float32)
        W_base = jax.random.normal(ks[1], (D_OUT, D_IN), dtype=jnp.float32) * (1.0 / np.sqrt(D_IN))
        b_base = jax.random.normal(ks[2], (D_OUT,), dtype=jnp.float32) * 0.01
        W_router = jax.random.normal(ks[3], (NUM_EXPERTS, D_IN), dtype=jnp.float32) * 0.01
        A_stack = jax.random.uniform(ks[4], (NUM_EXPERTS, RANK, D_IN), dtype=jnp.float32, minval=-1.0, maxval=1.0) * (1.0 / np.sqrt(D_IN))
        B_stack = jax.random.normal(ks[5], (NUM_EXPERTS, D_OUT, RANK), dtype=jnp.float32) * 0.02
        return {'x': x, 'W_base': W_base, 'b_base': b_base, 'W_router': W_router, 'A_stack': A_stack, 'B_stack': B_stack}
    _L0_ffn_all = _L0_ffn_setup()
    _L0_ffn_in = {k: v for k, v in _L0_ffn_all.items() if k in ('W_base', 'b_base', 'W_router', 'A_stack', 'B_stack')}
    del _L0_ffn_all
    return {'x': x, 'itok_B_3_7': itok_B_3_7, 'L0_cond_weight': _L0_cond_in['weight'], 'L0_ffn_W_base': _L0_ffn_in['W_base'], 'L0_ffn_b_base': _L0_ffn_in['b_base'], 'L0_ffn_W_router': _L0_ffn_in['W_router'], 'L0_ffn_A_stack': _L0_ffn_in['A_stack'], 'L0_ffn_B_stack': _L0_ffn_in['B_stack']}

def reference(x, itok_B_3_7, L0_cond_weight, L0_ffn_W_base, L0_ffn_b_base, L0_ffn_W_router, L0_ffn_A_stack, L0_ffn_B_stack):
    import jax
    import jax.numpy as jnp

    def _L0_cond_ref(x, weight, adapter_ids):
        import jax, jax.numpy as jnp
        import numpy as np
        MAX_LORAS, OUT, IN = (8, 1024, 1024)
        B, S = (4, 512)
        w = weight[adapter_ids]
        return jnp.einsum('bsi,boi->bso', x, w)

    def _L0_ffn_ref(x, W_base, b_base, W_router, A_stack, B_stack):
        import jax, jax.numpy as jnp
        import numpy as np
        D_IN = 1024
        D_OUT = 1024
        RANK = 16
        NUM_EXPERTS = 8
        TOP_K = 2
        SCALING = 32.0 / RANK
        orig_shape = x.shape
        xf = x.reshape(-1, D_IN)
        logits = xf @ W_router.T
        probs = jax.nn.softmax(logits, axis=-1)
        topk_p, topk_i = jax.lax.top_k(probs, TOP_K)
        topk_p = topk_p / jnp.sum(topk_p, axis=-1, keepdims=True)
        combine = jnp.sum(jax.nn.one_hot(topk_i, NUM_EXPERTS, dtype=xf.dtype) * topk_p[..., None], axis=1)
        h = jnp.einsum('nd,erd->ner', xf, A_stack)
        h = h * combine[..., None]
        lora_out = jnp.einsum('ner,eor->no', h, B_stack) * SCALING
        base_out = xf @ W_base.T + b_base
        out = base_out + lora_out
        return out.reshape(orig_shape[:-1] + (D_OUT,))
    x = x + _L0_ffn_ref(_L0_cond_ref(x, L0_cond_weight, itok_B_3_7), L0_ffn_W_base, L0_ffn_b_base, L0_ffn_W_router, L0_ffn_A_stack, L0_ffn_B_stack)
    return x

_drawn_inputs = setup_inputs


def setup_inputs(seed=0):
    import zlib

    import numpy as np

    out = dict(_drawn_inputs(seed))
    spreads = {}
    factors = {'L0_ffn_b_base': 6.611}
    for name, (base, spread) in spreads.items():
        noise = np.random.default_rng([zlib.crc32(name.encode()), seed]).standard_normal(out[name].shape)
        drawn = base * np.exp(spread * noise) if base else spread * noise
        out[name] = jnp.asarray(drawn.astype(out[name].dtype))
    for name, factor in factors.items():
        out[name] = (out[name] * factor).astype(out[name].dtype)
    return out
```

```python
from contextlib import ExitStack

import concourse.bass as bass
import numpy as np
from concourse import mybir
from concourse.alu_op_type import AluOpType as ALU

F32 = mybir.dt.float32
F32R = mybir.dt.float32r
ACT = mybir.ActivationFunctionType
AX = mybir.AxisListType

P = 128
SEQS, TOK, D = 8, 256, 1024
KT = D // P
EXPERTS, RANK = 8, 16
SCALING = 32.0 / RANK
PAIRS = SEQS // 2
PTOK = 2 * TOK
NQ = PTOK // P
SLOT = D
RAW = 4
WSLOTS = 4
BANKS = 4
OUTS = 2
HI, LO = 0, 1

C_ID, C_TRI, C_ALL = 0, P, P + EXPERTS * EXPERTS


def step_items(s, t):
    if t < 4:
        items = [("w", s, t + 4)]
        if t == 2:
            items.append(("x", s + 1, 0))
    else:
        items = [("w", s + 1, t - 4)]
        if t == 4:
            items.insert(0, ("x", s + 1, 1))
    return items


START = [("x", 0, 0), ("w", 0, 0), ("x", 0, 1)] + [("w", 0, t) for t in range(1, WSLOTS - 1)]
HALVES = [(0, 0), (1, 0), (0, 1), (2, 0), (1, 1), (2, 1), (3, 0), (3, 1)]
RESIDENT_COND = {(0, 5): [("a", 0, 0)], (1, 0): [("wb", 0, 0)]}
RESIDENT_BASE = {0: [("wb", 0, 1), ("b", 0, 0), ("wb", 0, 2)]} | {o: [("wb", 0, o + 2)] for o in range(1, KT - 2)}


def pair_stream(first, last):
    steps = []
    for s in range(2):
        for t in range(KT):
            items = [i for i in step_items(s, t) if not (last and i[1] == 2)]
            if first and (s, t) == (0, 0):
                items = [("w", 0, WSLOTS - 1)] + items
            if first:
                items = items + RESIDENT_COND.get((s, t), [])
            steps.append(((s, t), items))
    for o in range(KT):
        steps.append((("base", o), RESIDENT_BASE.get(o, []) if first else []))
    return steps


def build(nc, x, ids, w_cond, w_base, w_router, lora_a, lora_b, bias, consts, out):
    with ExitStack() as ctx:
        def sb(name, shape, dt=F32):
            return ctx.enter_context(nc.sbuf_tensor(name, shape, dt))

        def psum(name):
            return ctx.enter_context(nc.psum_tensor(name, [P, 512], F32))

        def sem(name):
            return ctx.enter_context(nc.semaphore(name))

        raw = sb("raw", [P, RAW, SLOT])
        x_hl = sb("x_hl", [P, 2, KT, 2, TOK], F32R)
        wc_hl = sb("wc_hl", [P, WSLOTS, 2, KT, P], F32R)
        wb_hl = sb("wb_hl", [P, KT, 2, KT, P], F32R)
        xc_hl = sb("xc_hl", [P, KT, 2, PTOK], F32R)
        a_hl = sb("a_hl", [P, 2, KT, P], F32R)
        b_hl = sb("b_hl", [P, 2, KT, P], F32R)
        NR = 2 * EXPERTS
        wr_raw = sb("wr_raw", [P, KT, EXPERTS])
        wr_hl = sb("wr_hl", [P, (KT - 1) * NR + P], F32R)
        wr_k = wr_hl[:, 0:KT * NR].rearrange("p (k n) -> p k n", n=NR)
        bias_sb = sb("bias_sb", [P, KT])
        const_sb = sb("const_sb", [P, C_ALL])
        out_sb = sb("out_sb", [P, OUTS, PTOK])
        h_sb = sb("h_sb", [P, PTOK])
        h_hl = sb("h_hl", [P, 2, PTOK], F32R)
        gate_er = sb("gate_er", [P, NQ, EXPERTS, RANK])
        logit_t = gate_er[0:NR].rearrange("p q e r -> p (q e r)")
        logit = sb("logit", [P, NQ, EXPERTS])
        shifted = sb("shifted", [P, NQ, EXPERTS])
        expd = sb("expd", [P, NQ, EXPERTS])
        probs = sb("probs", [P, NQ, EXPERTS])
        gate = sb("gate", [P, NQ, EXPERTS])
        rank = sb("rank", [P, NQ, EXPERTS])
        above = gate_er[:, :, :, 0:EXPERTS]
        xc_low = gate_er[:].rearrange("p q e r -> p (q e r)").rearrange("p (i n) -> p i n", i=2)
        xc_sum = h_sb[:].rearrange("p (i n) -> p i n", i=2)
        equal = gate_er[:, :, :, EXPERTS:2 * EXPERTS]
        stat = sb("stat", [P, 5, NQ])

        ident = const_sb[:, C_ID:C_ID + P]
        before = const_sb[:, C_TRI:C_TRI + EXPERTS * EXPERTS].rearrange("p (e j) -> p e j", e=EXPERTS)

        ps_base = [psum(f"ps_base{i}") for i in range(3)]
        ps_h = psum("ps_h")
        ps_logit = psum("ps_logit")
        ps_cond = [ps_logit, ps_h, psum("ps_cond2"), psum("ps_cond3")]
        ps_tok = psum("ps_tok")
        tok_parts = ps_tok[:, 0:NQ * NR].rearrange("p (q n) -> p q n", q=NQ)

        consts_in = sem("consts_in")
        bias_in = sem("bias_in")
        wr_in = sem("wr_in")
        raw_in = [sem(f"raw_in{i}") for i in range(RAW)]
        start_in = [sem(f"start_in{i}") for i in range(RAW)]
        start_hi = sem("start_hi")
        start_lo = sem("start_lo")
        hi_done = sem("hi_done")
        lo_done = sem("lo_done")
        wr_clear = sem("wr_clear")
        wr_hi = sem("wr_hi")
        wr_split = sem("wr_split")
        cond_done = sem("cond_done")
        low_copied = sem("low_copied")
        xc_summed = sem("xc_summed")
        xc_hi = sem("xc_hi")
        xc_lo = sem("xc_lo")
        router_done = sem("router_done")
        logit_copied = sem("logit_copied")
        tok_done = sem("tok_done")
        gate_step = sem("gate_step")
        exp_done = sem("exp_done")
        gate_ready = sem("gate_ready")
        gate_t_done = sem("gate_t_done")
        h_done = sem("h_done")
        h_copied = sem("h_copied")
        h_gated = sem("h_gated")
        h_hi = sem("h_hi")
        h_split = sem("h_split")
        base_done = sem("base_done")
        out_done = sem("out_done")
        res_in = [sem(f"res_in{i}") for i in range(OUTS)]
        stored = [sem(f"stored{i}") for i in range(OUTS)]

        block = ctx.enter_context(nc.Block())

        FIRST = pair_stream(True, False)
        AHEAD = [i for _, items in pair_stream(False, False) for i in items][:RAW]
        N_FIRST = len(START) + sum(len(i) for _, i in FIRST)
        N_PAIR = sum(len(i) for _, i in pair_stream(False, False))
        assert N_FIRST % RAW == 0 and N_PAIR % RAW == 0
        GATE_STEPS = 14

        class Stream:
            def __init__(self, p):
                self.n = 0
                if isinstance(p, int) and p == 0:
                    self.base, self.over = 0, 0
                else:
                    self.base = (p - 1) * N_PAIR + N_FIRST
                    self.over = (p - 1) * (N_PAIR // RAW) + N_FIRST // RAW

            def next(self):
                n, self.n = self.n, self.n + 1
                return self.base + n, n % RAW, self.over + n // RAW

        def split_dst(kind, d, t, hl):
            if kind == "w":
                return wc_hl[:, t % WSLOTS, hl]
            if kind == "x":
                return x_hl[:, d % 2, 4 * t:4 * t + 4, hl, :]
            if kind == "wb":
                return wb_hl[:, t, hl]
            return (a_hl if kind == "a" else b_hl)[:, hl]

        def raw_view(kind, slot):
            v = raw[:, slot]
            return v.rearrange("p (k n) -> p k n", n=TOK if kind == "x" else P)

        def half(v, h):
            n = v.shape[1] // 2
            return v[:, h * n:(h + 1) * n]

        def pairs(engine, body):
            body(0, True, False)
            with engine.Fori(1, PAIRS - 1) as p:
                body(p, False, False)
            body(PAIRS - 1, False, True)

        @block.sync
        def _(sp):
            def read_id(p, d):
                return nc.sync.value_load(ids[0:1, bass.ds(2 * p + d, 1)], min_val=0, max_val=w_cond.shape[0] - 1)

            def residual(p, o):
                src = x[bass.ds(2 * p, 2), o // 4, :, (o % 4) * TOK:(o % 4 + 1) * TOK].rearrange("b p n -> p b n")
                nc.sync.dma_start(out_sb[:, o % OUTS].rearrange("p (b n) -> p b n", b=2), src) \
                    .then_inc(res_in[o % OUTS], 16)

            def source(item, p, ids_of):
                kind, d, t = item
                if kind == "x":
                    return x[bass.ds(2 * p + d, 1), t, :, :].rearrange("a p n -> (a p) n")
                if kind == "w":
                    return w_cond[bass.ds(ids_of[d], 1), t, :, :].rearrange("a p n -> (a p) n")
                return w_base[t] if kind == "wb" else lora_a if kind == "a" else lora_b

            def load(item, p, ids_of, place):
                n, slot, _ = place
                if not (isinstance(n, int) and n < RAW):
                    sp.wait_ge(lo_done, n - RAW + 1)
                nc.sync.dma_start(raw[:, slot], source(item, p, ids_of)).then_inc(raw_in[slot], 16)

            def load_start(ids_of):
                for i, h in HALVES:
                    if START[i][0] == "w" and not ids_of:
                        ids_of.append(read_id(0, 0))
                    n = SLOT // 2
                    nc.sync.dma_start(raw[:, i, h * n:(h + 1) * n], source(START[i], 0, ids_of)[:, h * n:(h + 1) * n]) \
                        .then_inc(raw_in[i] if h else start_in[i], 16)

            def body(p, first, last):
                places = Stream(p)
                steps = pair_stream(first, last)
                cond_items = [i for st, items in steps for i in items if st[0] != "base"]
                ahead = [i for st, items in steps for i in items if st[0] == "base"]
                if not last:
                    ahead += [(kind, d + 2, t) for kind, d, t in AHEAD]
                if first:
                    ids_of = []
                    load_start(ids_of)
                    for _ in range(RAW):
                        places.next()
                    for item in START[RAW:]:
                        load(item, p, ids_of, places.next())
                else:
                    ids_of = [read_id(p, d) for d in range(2 if last else 3)]
                    for _ in range(RAW):
                        places.next()
                    cond_items = cond_items[RAW:]
                for item in cond_items + ahead[:RAW]:
                    if item[0] == "w" and item[1] >= len(ids_of):
                        ids_of.append(read_id(p, item[1]))
                    load(item, p, ids_of, places.next())
                for o in range(OUTS):
                    if not first:
                        sp.wait_ge(stored[o], 16 * (KT // OUTS) * p)
                    residual(p, o)
                for o in range(KT):
                    for item in ahead[RAW + o:RAW + o + 1]:
                        load(item, p, ids_of, places.next())
                    sp.wait_ge(out_done, p * KT + o + 1)
                    nc.sync.dma_start(out[bass.ds(p, 1), o].rearrange("a p n -> (a p) n"),
                                      out_sb[:, o % OUTS]).then_inc(stored[o % OUTS], 16)
                    if o + OUTS < KT:
                        sp.wait_ge(stored[o % OUTS], p * (16 * (KT // OUTS)) + 16 * (o // OUTS + 1))
                        residual(p, o + OUTS)

            pairs(sp, body)
            for o in range(OUTS):
                sp.wait_ge(stored[o], 16 * (KT // OUTS) * PAIRS)

        @block.gpsimd
        def _(pool):
            nc.gpsimd.dma_start(wr_raw[:], w_router).then_inc(wr_in, 16)
            nc.gpsimd.dma_start(const_sb[:], consts).then_inc(consts_in, 16)
            nc.gpsimd.dma_start(bias_sb[:], bias).then_inc(bias_in, 16)

        @block.scalar
        def _(act):
            def split_hi(items, places):
                for kind, d, t in items:
                    _, slot, over = places.next()
                    act.wait_ge(raw_in[slot], (over + 1) * 16)
                    nc.scalar.copy(split_dst(kind, d, t, HI), raw_view(kind, slot)).then_inc(hi_done, 1)

            def body(p, first, last):
                places = Stream(p)
                if first:
                    for i, h in HALVES:
                        act.wait_ge(raw_in[i] if h else start_in[i], 16)
                        nc.scalar.copy(half(split_dst(*START[i], HI), h), half(raw_view(START[i][0], i), h)) \
                            .then_inc(hi_done if h else start_hi, 1)
                    for _ in range(RAW):
                        places.next()
                    split_hi(START[RAW:], places)
                for step, items in pair_stream(first, last):
                    if step[0] == "base":
                        if step[1] == 0:
                            act.wait_ge(router_done, p + 1)
                            nc.scalar.copy(logit_t, ps_logit[0:NR, :]).then_inc(logit_copied, 1)
                            act.wait_ge(gate_step, p * GATE_STEPS + 3)
                            nc.scalar.activation(expd[:], shifted[:], ACT.Exp).then_inc(exp_done, 1)
                            act.wait_ge(h_done, p + 1)
                            if not first:
                                act.wait_ge(h_split, p)
                            nc.scalar.copy(h_sb[:], ps_h[:]).then_inc(h_copied, 1)
                        split_hi(items, places)
                        if step[1] == 0:
                            act.wait_ge(h_gated, p + 1)
                            nc.scalar.copy(h_hl[:, HI], h_sb[:]).then_inc(h_hi, 1)
                        continue
                    s, t = step
                    if first and step == (1, 0):
                        act.wait_ge(wr_in, 16)
                        act.wait_ge(wr_clear, 1)
                        nc.scalar.copy(wr_k[:, :, 0:EXPERTS], wr_raw[:]).then_inc(wr_hi, 1)
                    act.wait_ge(cond_done, p * (2 * KT) + s * KT + t + 1)
                    nc.scalar.copy(xc_low[:, t % 2], ps_cond[t % BANKS][:, TOK:]).then_inc(low_copied, 1)
                    if t < KT - 2:
                        split_hi(items, places)
                    act.wait_ge(xc_summed, p * (2 * KT) + s * KT + t + 1)
                    nc.scalar.copy(xc_hl[:, t, HI, s * TOK:(s + 1) * TOK], xc_sum[:, t % 2]).then_inc(xc_hi, 1)
                    if t >= KT - 2:
                        split_hi(items, places)

            pairs(act, body)

        @block.vector
        def _(dve):
            nc.vector.memset(wr_hl[:].bitcast(F32), 0.0).then_inc(wr_clear, 1)

            def split_lo(items, places):
                for kind, d, t in items:
                    n, slot, _ = places.next()
                    dve.wait_ge(hi_done, n + 1)
                    nc.vector.tensor_tensor(split_dst(kind, d, t, LO), raw_view(kind, slot),
                                            split_dst(kind, d, t, HI).bitcast(F32), ALU.subtract) \
                        .then_inc(lo_done, 1)

            def make_gate(p):
                mx, total, inv, two, inv2 = (stat[:, i] for i in range(5))
                at = [0]

                def chain(ins):
                    at[0] += 1
                    ins.then_inc(gate_step, 1)

                def ready():
                    dve.wait_ge(gate_step, p * GATE_STEPS + at[0])

                def per_token(s):
                    return s[:, :, None].broadcast_to([P, NQ, EXPERTS])

                v4 = [P, NQ, EXPERTS, EXPERTS]
                dve.wait_ge(tok_done, p + 1)
                chain(nc.vector.tensor_reduce(logit[:], tok_parts.rearrange("p q (h e) -> p q e h", h=2), AX.X,
                                              ALU.add))
                ready()
                chain(nc.vector.tensor_reduce(mx, logit[:], AX.X, ALU.max))
                ready()
                chain(nc.vector.tensor_tensor(shifted[:], logit[:], per_token(mx), ALU.subtract))
                dve.wait_ge(exp_done, p + 1)
                chain(nc.vector.tensor_reduce(total, expd[:], AX.X, ALU.add))
                ready()
                chain(nc.vector.reciprocal(inv, total))
                ready()
                chain(nc.vector.tensor_tensor(probs[:], expd[:], per_token(inv), ALU.mult))
                ready()
                of_j = probs[:, :, None, :].broadcast_to(v4)
                of_e = probs[:, :, :, None].broadcast_to(v4)
                nc.vector.tensor_tensor(above, of_j, of_e, ALU.is_gt)
                chain(nc.vector.tensor_tensor(equal, of_j, of_e, ALU.is_equal))
                ready()
                if isinstance(p, int) and p == 0:
                    dve.wait_ge(consts_in, 16)
                for_q = before[:, None].broadcast_to(v4)
                chain(nc.vector.tensor_tensor(equal, equal, for_q, ALU.mult))
                ready()
                chain(nc.vector.tensor_tensor(above, above, equal, ALU.add))
                ready()
                chain(nc.vector.tensor_reduce(rank[:], above, AX.X, ALU.add))
                ready()
                chain(nc.vector.scalar_tensor_tensor(gate[:], rank[:], 2.0, probs[:], ALU.is_lt, ALU.mult))
                ready()
                chain(nc.vector.tensor_reduce(two, gate[:], AX.X, ALU.add))
                ready()
                chain(nc.vector.reciprocal(inv2, two))
                ready()
                nc.vector.scalar_tensor_tensor(gate[:], gate[:], SCALING, per_token(inv2), ALU.mult, ALU.mult) \
                    .then_inc(gate_step, 1)
                at[0] += 1
                ready()
                assert at[0] == GATE_STEPS
                nc.vector.tensor_copy(gate_er[:], gate[:, :, :, None].broadcast_to([P, NQ, EXPERTS, RANK])) \
                    .then_inc(gate_ready, 1)

            def body(p, first, last):
                places = Stream(p)
                if first:
                    done = [0, 0]
                    for i, h in HALVES:
                        done[h] += 1
                        dve.wait_ge(hi_done if h else start_hi, done[h])
                        nc.vector.tensor_tensor(half(split_dst(*START[i], LO), h), half(raw_view(START[i][0], i), h),
                                                half(split_dst(*START[i], HI), h).bitcast(F32), ALU.subtract) \
                            .then_inc(lo_done if h else start_lo, 1)
                    for _ in range(RAW):
                        places.next()
                    split_lo(START[RAW:], places)
                for step, items in pair_stream(first, last):
                    if step[0] == "base":
                        o = step[1]
                        if first and o == 0:
                            dve.wait_ge(bias_in, 16)
                        if o == 0:
                            make_gate(p)
                        split_lo(items, places)
                        if o == 0:
                            dve.wait_ge(gate_t_done, p + 1)
                            dve.wait_ge(h_copied, p + 1)
                            nc.vector.tensor_tensor(h_sb[:], h_sb[:], ps_tok[:], ALU.mult).then_inc(h_gated, 1)
                            dve.wait_ge(h_hi, p + 1)
                            nc.vector.tensor_tensor(h_hl[:, LO], h_sb[:], h_hl[:, HI].bitcast(F32), ALU.subtract) \
                                .then_inc(h_split, 1)
                        dve.wait_ge(base_done, p * KT + o + 1)
                        dve.wait_ge(res_in[o % OUTS], p * (16 * (KT // OUTS)) + 16 * (o // OUTS + 1))
                        nc.vector.scalar_tensor_tensor(out_sb[:, o % OUTS], ps_base[o % 3][:], bias_sb[:, o:o + 1],
                                                       out_sb[:, o % OUTS], ALU.add, ALU.add).then_inc(out_done, 1)
                        continue
                    s, t = step
                    if first and step == (1, 0):
                        dve.wait_ge(wr_hi, 1)
                        nc.vector.tensor_tensor(wr_k[:, :, EXPERTS:NR], wr_raw[:],
                                                wr_k[:, :, 0:EXPERTS].bitcast(F32), ALU.subtract) \
                            .then_inc(wr_split, 1)
                    c = p * (2 * KT) + s * KT + t + 1
                    dve.wait_ge(low_copied, c)
                    nc.vector.tensor_tensor(xc_sum[:, t % 2], ps_cond[t % BANKS][:, 0:TOK], xc_low[:, t % 2], ALU.add) \
                        .then_inc(xc_summed, 1)
                    if t < KT - 2:
                        split_lo(items, places)
                    dve.wait_ge(xc_hi, c)
                    nc.vector.tensor_tensor(xc_hl[:, t, LO, s * TOK:(s + 1) * TOK], xc_sum[:, t % 2],
                                            xc_hl[:, t, HI, s * TOK:(s + 1) * TOK].bitcast(F32), ALU.subtract) \
                        .then_inc(xc_lo, 1)
                    if t >= KT - 2:
                        split_lo(items, places)

            pairs(dve, body)

        @block.tensor
        def _(pe):
            def product(ps, w_hi, w_lo, v_hi, v_lo, start, stop):
                nc.tensor.matmul(ps, w_hi, v_hi, start=start, stop=False)
                nc.tensor.matmul(ps, w_hi, v_lo, start=False, stop=False)
                return nc.tensor.matmul(ps, w_lo, v_hi, start=False, stop=stop)

            def cond(p, first, s):
                for t in range(KT):
                    c = p * (2 * KT) + s * KT + t
                    key = ("w", s, t)
                    start = first and s == 0 and t < 2
                    if key in split_at and not start:
                        pe.wait_ge(lo_done, split_at[key] + 1)
                    if t == 0 and ("x", s, 1) in split_at and not start:
                        pe.wait_ge(lo_done, split_at[("x", s, 1)] + 1)
                    if not (first and s == 0 and t < BANKS):
                        pe.wait_ge(xc_summed, c - BANKS + 1)
                    w, ps = t % WSLOTS, ps_cond[t % BANKS]
                    for k in range(KT):
                        if start and t == 0:
                            if k == 0:
                                pe.wait_ge(start_lo, 2)
                            if k == 2:
                                pe.wait_ge(lo_done, 1)
                            if k == 4:
                                pe.wait_ge(start_lo, 3)
                                pe.wait_ge(lo_done, 2)
                            if k == 6:
                                pe.wait_ge(lo_done, 3)
                        if start and t == 1:
                            if k == 0:
                                pe.wait_ge(start_lo, 4)
                            if k == 4:
                                pe.wait_ge(lo_done, 4)
                        nc.tensor.matmul(ps[:], wc_hl[:, w, HI, k], x_hl[:, s, k].rearrange("p h n -> p (h n)"),
                                         start=(k == 0), stop=False)
                        mm = nc.tensor.matmul(ps[:, TOK:], wc_hl[:, w, LO, k], x_hl[:, s, k, HI],
                                              start=False, stop=(k == KT - 1))
                    mm.then_inc(cond_done, 1)

            def router(p, first):
                if first:
                    pe.wait_ge(wr_split, 1)
                for k in range(KT):
                    if k == 0 or k == KT - 1:
                        pe.wait_ge(xc_lo, p * (2 * KT) + KT + (KT - 1 if k == 0 else KT))
                    w = wr_hl[:, k * NR:k * NR + P]
                    nc.tensor.matmul(ps_logit[:], w, xc_hl[:, k, HI], start=(k == 0), stop=False)
                    mm = nc.tensor.matmul(ps_logit[:], w, xc_hl[:, k, LO], start=False, stop=(k == KT - 1))
                mm.then_inc(router_done, 1)

            def lora_down(p, first):
                if first:
                    pe.wait_ge(lo_done, split_at[("a", 0, 0)] + 1)
                for k in range(KT):
                    if k == KT // 2:
                        pe.wait_ge(logit_copied, p + 1)
                        if first:
                            pe.wait_ge(consts_in, 16)
                    mm = product(ps_h[:], a_hl[:, HI, k], a_hl[:, LO, k], xc_hl[:, k, HI], xc_hl[:, k, LO],
                                 k == 0, k == KT - 1)
                    if k == KT // 2:
                        for q in range(NQ):
                            tok = nc.tensor.transpose(tok_parts[:, q], logit_t[:, q * P:(q + 1) * P],
                                                      ident[0:NR, 0:NR])
                        tok.then_inc(tok_done, 1)
                mm.then_inc(h_done, 1)

            def base(p, first, o):
                if first:
                    pe.wait_ge(lo_done, split_at[("wb", 0, o)] + 1)
                if not first and o == 0:
                    pe.wait_ge(out_done, p * KT)
                if o >= 3:
                    pe.wait_ge(out_done, p * KT + o - 2)
                for k in range(KT):
                    product(ps_base[o % 3][:], wb_hl[:, o, HI, k], wb_hl[:, o, LO, k],
                            xc_hl[:, k, HI], xc_hl[:, k, LO], k == 0, False)

            def lora_up(o):
                product(ps_base[o % 3][:], b_hl[:, HI, o], b_hl[:, LO, o], h_hl[:, HI], h_hl[:, LO],
                        False, True).then_inc(base_done, 1)

            split_at = {}

            def body(p, first, last):
                split_at.clear()
                places = Stream(p)
                for item in (START if first else []) + [i for _, s in pair_stream(first, last) for i in s]:
                    split_at[item] = places.next()[0]
                if not first:
                    pe.wait_ge(lo_done, places.base)
                cond(p, first, 0)
                cond(p, first, 1)
                router(p, first)
                lora_down(p, first)
                base(p, first, 0)
                pe.wait_ge(gate_ready, p + 1)
                for q in range(NQ):
                    tr = nc.tensor.transpose(ps_tok[:, q * P:(q + 1) * P],
                                             gate_er[:, q].rearrange("p e r -> p (e r)"), ident)
                tr.then_inc(gate_t_done, 1)
                for o in range(1, KT):
                    base(p, first, o)
                    if o == 1:
                        if first:
                            pe.wait_ge(lo_done, split_at[("b", 0, 0)] + 1)
                        pe.wait_ge(h_split, p + 1)
                    lora_up(o - 1)
                lora_up(KT - 1)

            pairs(pe, body)


def kernel(x, itok_B_3_7, L0_cond_weight, L0_ffn_W_base, L0_ffn_b_base, L0_ffn_W_router, L0_ffn_A_stack,
           L0_ffn_B_stack):
    import concourse.bacc as bacc
    from concourse.bass_utils import run_bass_kernel_spmd

    def tiles(w):
        v = np.asarray(w).reshape(w.shape[:-2] + (KT, P, KT, P))
        return np.ascontiguousarray(np.moveaxis(v, (-4, -1, -2, -3), (-4, -3, -2, -1))).reshape(
            w.shape[:-2] + (KT, P, D))

    e = np.arange(EXPERTS)
    consts = np.zeros((P, C_ALL), np.float32)
    consts[:, C_ID:C_ID + P] = np.eye(P)
    consts[:, C_TRI:C_TRI + EXPERTS * EXPERTS] = (e[None, :] < e[:, None]).reshape(1, -1)

    x_t = np.asarray(x).reshape(SEQS, TOK, 2, KT // 2, P).transpose(0, 2, 4, 3, 1)
    a_t = np.asarray(L0_ffn_A_stack).reshape(P, KT, P).transpose(2, 1, 0)
    b_t = np.asarray(L0_ffn_B_stack).transpose(0, 2, 1)
    arrays = {
        "x": x_t.reshape(SEQS, 2, P, D),
        "ids": np.asarray(itok_B_3_7).reshape(1, SEQS),
        "w_cond": tiles(L0_cond_weight),
        "w_base": tiles(L0_ffn_W_base),
        "w_router": np.asarray(L0_ffn_W_router).reshape(EXPERTS, KT, P).transpose(2, 1, 0),
        "lora_a": a_t.reshape(P, D),
        "lora_b": b_t.reshape(P, D),
        "bias": np.asarray(L0_ffn_b_base).reshape(KT, P).T,
        "consts": consts,
    }
    arrays = {n: np.ascontiguousarray(a) for n, a in arrays.items()}
    nc = bacc.Bacc("TRN2", target_bir_lowering=False, num_devices=1)
    args = [nc.dram_tensor(n, a.shape, mybir.dt.from_np(a.dtype), kind="ExternalInput").ap()
            for n, a in arrays.items()]
    out = nc.dram_tensor("out", (PAIRS, KT, P, PTOK), F32, kind="ExternalOutput").ap()
    build(nc, *args, out)
    got = run_bass_kernel_spmd(nc, [arrays], core_ids=[0]).results[0]["out"]
    return got.reshape(PAIRS, KT, P, 2, TOK).transpose(0, 3, 4, 1, 2).reshape(SEQS, TOK, D)
```
